# Optimizing a Trainium2 kernel written in Bass

```python
import numpy as np
import jax
import jax.numpy as jnp

def _softmax(x, axis=-1):
    return jax.nn.softmax(x, axis=axis)

def _gelu(x):
    return jax.nn.gelu(x, approximate=True)

def _silu(x):
    return jax.nn.silu(x)

def _sigmoid(x):
    return jax.nn.sigmoid(x)

def _layernorm(x, axis=-1, eps=1e-05):
    m = jnp.mean(x, axis=axis, keepdims=True)
    v = jnp.var(x, axis=axis, keepdims=True)
    return (x - m) / jnp.sqrt(v + eps)

def _scatter_add(tgt, idx, src, axis=0):
    return tgt.at[idx].add(src)

def _segment_sum(src, seg, n):
    return jax.ops.segment_sum(src, seg, n)
kernel_name = 'mk_seq_preln_d1_jaxref_r8_df835b'

def setup_inputs(seed: int=0):
    np.random.seed(seed)
    _w = jnp.asarray

    def _L0_attn_setup():
        import jax, jax.numpy as jnp
        import numpy as np
        B, N, D, H = (2, 128, 128, 16)
        DH = D // H
        SCALE = 1.0 / DH ** 0.5
        STJ_Q = 1.0
        NUM_ITER = 4
        CAUSAL = True
        EPS = 1e-06

        def stieltjes_attention(Q, K, V, scale, causal, q, num_iter):
            n = Q.shape[2]
            s = jnp.einsum('bhnd,bhmd->bhnm', Q, K) * scale
            if causal:
                mask = jnp.tril(jnp.ones((n, n), bool))
            else:
                mask = jnp.ones((n, n), bool)
            s_masked = jnp.where(mask, s, -1e+30)
            lam = s_masked.max(-1) + 1.0
            for _ in range(num_iter):
                d = jnp.maximum(lam[..., None] - s, EPS)
                w = jnp.where(mask, d ** (-q), 0.0)
                f = w.sum(-1) - 1.0
                fp = -q * jnp.where(mask, d ** (-q - 1.0), 0.0).sum(-1)
                lam = lam - f / fp
            d = jnp.maximum(lam[..., None] - s, EPS)
            p = jnp.where(mask, d ** (-q), 0.0)
            p = p / p.sum(-1, keepdims=True)
            return jnp.einsum('bhnm,bhmd->bhnd', p, V)
        key = jax.random.key(seed)
        k1, k2, k3 = jax.random.split(key, 3)
        x = jax.random.normal(k1, (B, N, D), jnp.float32)
        Wqkv = jax.random.normal(k2, (3 * D, D), jnp.float32) / np.float32(np.sqrt(D))
        Wo = jax.random.normal(k3, (D, D), jnp.float32) / np.float32(np.sqrt(D))
        return {'x': x, 'Wqkv': Wqkv, 'Wo': Wo}
    _L0_attn_in = _L0_attn_setup()

    def _L0_ffn_setup():
        import jax, jax.numpy as jnp
        import numpy as np
        DIM = 128
        DEPTH = 6
        HEADS = 16
        DIM_HEAD = 64
        WINDOW = 32
        INNER = HEADS * DIM_HEAD
        DIM_INNER = int(DIM * 4 * 2 / 3)
        QK_SCALE = 8.0

        def shift_tokens(t):
            a, s = jnp.split(t, 2, -1)
            s = jnp.pad(s, ((0, 0), (1, 0), (0, 0)))[:, :-1]
            return jnp.concatenate([a, s], -1)

        def l2norm(t):
            return t / jnp.maximum(jnp.linalg.norm(t, axis=-1, keepdims=True), 1e-12)

        def rotate_half(x):
            x1, x2 = jnp.split(x, 2, -1)
            return jnp.concatenate([-x2, x1], -1)

        def rotary_tables(n):
            half = jnp.arange(0, DIM_HEAD, 2, dtype=jnp.float32)
            inv_freq = 1.0 / 10000.0 ** (half / DIM_HEAD)
            t = jnp.arange(n, dtype=jnp.float32)
            freqs = t[:, None] * inv_freq[None, :]
            freqs = jnp.concatenate([freqs, freqs], -1)
            base_scale = (half + 0.4 * DIM_HEAD) / (1.4 * DIM_HEAD)
            power = (t - n // 2) / (WINDOW // 2)
            scale = base_scale[None, :] ** power[:, None]
            scale = jnp.concatenate([scale, scale], -1)
            return (freqs, scale)

        def local_attention(q, k, v):
            b, h, n, d = q.shape
            w = WINDOW
            nw = n // w
            bq = q.reshape(b, h, nw, w, d)
            bk = k.reshape(b, h, nw, w, d)
            bv = v.reshape(b, h, nw, w, d)

            def look(t):
                p = jnp.pad(t, ((0, 0), (0, 0), (1, 0), (0, 0), (0, 0)))
                return jnp.concatenate([p[:, :, :nw], p[:, :, 1:]], axis=3)
            bk2, bv2 = (look(bk), look(bv))
            seq = jnp.arange(n).reshape(nw, w)
            seq_p = jnp.pad(seq, ((1, 0), (0, 0)), constant_values=-1)
            jt = jnp.concatenate([seq_p[:nw], seq_p[1:]], axis=1)
            it = seq[:, :, None]
            jb = jt[:, None, :]
            mask = (it < jb) | (it > jb + w) | (jb == -1)
            sim = jnp.einsum('bhwie,bhwje->bhwij', bq, bk2) * QK_SCALE
            sim = jnp.where(mask, -jnp.finfo(sim.dtype).max, sim)
            attn = jax.nn.softmax(sim, -1)
            out = jnp.einsum('bhwij,bhwje->bhwie', attn, bv2)
            return out.reshape(b, h, n, d)

        def attn_layer(x, Wqkv, qs, ksc, Wo):
            b, n, _ = x.shape
            qkv = x @ Wqkv
            q, k, v = jnp.split(qkv, 3, -1)
            sh = lambda t: t.reshape(b, n, HEADS, DIM_HEAD).transpose(0, 2, 1, 3)
            q, k, v = (sh(q), sh(k), sh(v))
            q = l2norm(q) * qs
            k = l2norm(k) * ksc
            freqs, scale = rotary_tables(n)
            cos, sin = (jnp.cos(freqs), jnp.sin(freqs))
            q = q * cos * scale + rotate_half(q) * sin * scale
            inv = 1.0 / scale
            k = k * cos * inv + rotate_half(k) * sin * inv
            out = local_attention(q, k, v)
            out = out.transpose(0, 2, 1, 3).reshape(b, n, INNER)
            return out @ Wo

        def ffn_layer(x, g, bln, W1, b1, W2, b2):
            mu = x.mean(-1, keepdims=True)
            var = ((x - mu) ** 2).mean(-1, keepdims=True)
            xn = (x - mu) / jnp.sqrt(var + 1e-05) * g + bln
            hg = xn @ W1 + b1
            a, gate = jnp.split(hg, 2, -1)
            return a * jax.nn.gelu(gate, approximate=False) @ W2 + b2
        key = jax.random.key(seed)
        ks = jax.random.split(key, 8)
        B, N = (2, 256)
        init = lambda k, shape: jax.random.normal(k, shape, jnp.float32) * 0.02
        return {'x': jax.random.normal(ks[0], (B, N, DIM), jnp.float32), 'Wqkv': init(ks[1], (DEPTH, DIM, 3 * INNER)), 'q_scale': jnp.ones((DEPTH, DIM_HEAD), jnp.float32), 'k_scale': jnp.ones((DEPTH, DIM_HEAD), jnp.float32), 'Wo': init(ks[2], (DEPTH, INNER, DIM)), 'ln_g': jnp.ones((DEPTH, DIM), jnp.float32), 'ln_b': jnp.zeros((DEPTH, DIM), jnp.float32), 'W1': init(ks[3], (DEPTH, DIM, 2 * DIM_INNER)), 'b1': jnp.zeros((DEPTH, 2 * DIM_INNER), jnp.float32), 'W2': init(ks[4], (DEPTH, DIM_INNER, DIM)), 'b2': jnp.zeros((DEPTH, DIM), jnp.float32)}
    _L0_ffn_in = _L0_ffn_setup()
    _d = {'L0_attn_x': _L0_attn_in['x'], 'L0_attn_Wqkv': _L0_attn_in['Wqkv'], 'L0_attn_Wo': _L0_attn_in['Wo'], 'L0_ffn_Wqkv': _L0_ffn_in['Wqkv'], 'L0_ffn_q_scale': _L0_ffn_in['q_scale'], 'L0_ffn_k_scale': _L0_ffn_in['k_scale'], 'L0_ffn_Wo': _L0_ffn_in['Wo'], 'L0_ffn_ln_g': _L0_ffn_in['ln_g'], 'L0_ffn_ln_b': _L0_ffn_in['ln_b'], 'L0_ffn_W1': _L0_ffn_in['W1'], 'L0_ffn_b1': _L0_ffn_in['b1'], 'L0_ffn_W2': _L0_ffn_in['W2'], 'L0_ffn_b2': _L0_ffn_in['b2']}
    _x0 = _d['L0_attn_x']
    _d['L0_attn_x'] = jax.random.normal(jax.random.fold_in(jax.random.key(seed), 1), (8, 512, 128), dtype=_x0.dtype)
    del _x0
    return _d

def reference(L0_attn_x, L0_attn_Wqkv, L0_attn_Wo, L0_ffn_Wqkv, L0_ffn_q_scale, L0_ffn_k_scale, L0_ffn_Wo, L0_ffn_ln_g, L0_ffn_ln_b, L0_ffn_W1, L0_ffn_b1, L0_ffn_W2, L0_ffn_b2):

    def _L0_attn_ref(x, Wqkv, Wo):
        import jax, jax.numpy as jnp
        import numpy as np
        B, N, D, H = (2, 128, 128, 16)
        DH = D // H
        SCALE = 1.0 / DH ** 0.5
        STJ_Q = 1.0
        NUM_ITER = 4
        CAUSAL = True
        EPS = 1e-06

        def stieltjes_attention(Q, K, V, scale, causal, q, num_iter):
            n = Q.shape[2]
            s = jnp.einsum('bhnd,bhmd->bhnm', Q, K) * scale
            if causal:
                mask = jnp.tril(jnp.ones((n, n), bool))
            else:
                mask = jnp.ones((n, n), bool)
            s_masked = jnp.where(mask, s, -1e+30)
            lam = s_masked.max(-1) + 1.0
            for _ in range(num_iter):
                d = jnp.maximum(lam[..., None] - s, EPS)
                w = jnp.where(mask, d ** (-q), 0.0)
                f = w.sum(-1) - 1.0
                fp = -q * jnp.where(mask, d ** (-q - 1.0), 0.0).sum(-1)
                lam = lam - f / fp
            d = jnp.maximum(lam[..., None] - s, EPS)
            p = jnp.where(mask, d ** (-q), 0.0)
            p = p / p.sum(-1, keepdims=True)
            return jnp.einsum('bhnm,bhmd->bhnd', p, V)
        b, n, dmodel = x.shape
        qkv = (x @ Wqkv.T).reshape(b, n, 3, H, DH).transpose(2, 0, 3, 1, 4)
        Q, K, V = (qkv[0], qkv[1], qkv[2])
        o = stieltjes_attention(Q, K, V, SCALE, CAUSAL, STJ_Q, NUM_ITER)
        o = o.transpose(0, 2, 1, 3).reshape(b, n, dmodel)
        return o @ Wo.T

    def _L0_ffn_ref(x, Wqkv, q_scale, k_scale, Wo, ln_g, ln_b, W1, b1, W2, b2):
        import jax, jax.numpy as jnp
        import numpy as np
        DIM = 128
        DEPTH = 6
        HEADS = 16
        DIM_HEAD = 64
        WINDOW = 32
        INNER = HEADS * DIM_HEAD
        DIM_INNER = int(DIM * 4 * 2 / 3)
        QK_SCALE = 8.0

        def shift_tokens(t):
            a, s = jnp.split(t, 2, -1)
            s = jnp.pad(s, ((0, 0), (1, 0), (0, 0)))[:, :-1]
            return jnp.concatenate([a, s], -1)

        def l2norm(t):
            return t / jnp.maximum(jnp.linalg.norm(t, axis=-1, keepdims=True), 1e-12)

        def rotate_half(x):
            x1, x2 = jnp.split(x, 2, -1)
            return jnp.concatenate([-x2, x1], -1)

        def rotary_tables(n):
            half = jnp.arange(0, DIM_HEAD, 2, dtype=jnp.float32)
            inv_freq = 1.0 / 10000.0 ** (half / DIM_HEAD)
            t = jnp.arange(n, dtype=jnp.float32)
            freqs = t[:, None] * inv_freq[None, :]
            freqs = jnp.concatenate([freqs, freqs], -1)
            base_scale = (half + 0.4 * DIM_HEAD) / (1.4 * DIM_HEAD)
            power = (t - n // 2) / (WINDOW // 2)
            scale = base_scale[None, :] ** power[:, None]
            scale = jnp.concatenate([scale, scale], -1)
            return (freqs, scale)

        def local_attention(q, k, v):
            b, h, n, d = q.shape
            w = WINDOW
            nw = n // w
            bq = q.reshape(b, h, nw, w, d)
            bk = k.reshape(b, h, nw, w, d)
            bv = v.reshape(b, h, nw, w, d)

            def look(t):
                p = jnp.pad(t, ((0, 0), (0, 0), (1, 0), (0, 0), (0, 0)))
                return jnp.concatenate([p[:, :, :nw], p[:, :, 1:]], axis=3)
            bk2, bv2 = (look(bk), look(bv))
            seq = jnp.arange(n).reshape(nw, w)
            seq_p = jnp.pad(seq, ((1, 0), (0, 0)), constant_values=-1)
            jt = jnp.concatenate([seq_p[:nw], seq_p[1:]], axis=1)
            it = seq[:, :, None]
            jb = jt[:, None, :]
            mask = (it < jb) | (it > jb + w) | (jb == -1)
            sim = jnp.einsum('bhwie,bhwje->bhwij', bq, bk2) * QK_SCALE
            sim = jnp.where(mask, -jnp.finfo(sim.dtype).max, sim)
            attn = jax.nn.softmax(sim, -1)
            out = jnp.einsum('bhwij,bhwje->bhwie', attn, bv2)
            return out.reshape(b, h, n, d)

        def attn_layer(x, Wqkv, qs, ksc, Wo):
            b, n, _ = x.shape
            qkv = x @ Wqkv
            q, k, v = jnp.split(qkv, 3, -1)
            sh = lambda t: t.reshape(b, n, HEADS, DIM_HEAD).transpose(0, 2, 1, 3)
            q, k, v = (sh(q), sh(k), sh(v))
            q = l2norm(q) * qs
            k = l2norm(k) * ksc
            freqs, scale = rotary_tables(n)
            cos, sin = (jnp.cos(freqs), jnp.sin(freqs))
            q = q * cos * scale + rotate_half(q) * sin * scale
            inv = 1.0 / scale
            k = k * cos * inv + rotate_half(k) * sin * inv
            out = local_attention(q, k, v)
            out = out.transpose(0, 2, 1, 3).reshape(b, n, INNER)
            return out @ Wo

        def ffn_layer(x, g, bln, W1, b1, W2, b2):
            mu = x.mean(-1, keepdims=True)
            var = ((x - mu) ** 2).mean(-1, keepdims=True)
            xn = (x - mu) / jnp.sqrt(var + 1e-05) * g + bln
            hg = xn @ W1 + b1
            a, gate = jnp.split(hg, 2, -1)
            return a * jax.nn.gelu(gate, approximate=False) @ W2 + b2
        for i in range(DEPTH):
            x = attn_layer(shift_tokens(x), Wqkv[i], q_scale[i], k_scale[i], Wo[i]) + x
            x = ffn_layer(shift_tokens(x), ln_g[i], ln_b[i], W1[i], b1[i], W2[i], b2[i]) + x
        return x
    x = L0_attn_x
    x = x + _L0_attn_ref(_layernorm(x, axis=-1), L0_attn_Wqkv, L0_attn_Wo)
    x = x + _L0_ffn_ref(_layernorm(x, axis=-1), L0_ffn_Wqkv, L0_ffn_q_scale, L0_ffn_k_scale, L0_ffn_Wo, L0_ffn_ln_g, L0_ffn_ln_b, L0_ffn_W1, L0_ffn_b1, L0_ffn_W2, L0_ffn_b2)
    return x

_drawn_inputs = setup_inputs


def setup_inputs(seed=0):
    import zlib

    import numpy as np

    out = dict(_drawn_inputs(seed))
    spreads = {'L0_ffn_q_scale': (1.0, 0.6),
     'L0_ffn_k_scale': (1.0, 0.6),
     'L0_ffn_ln_g': (1.0, 0.6),
     'L0_ffn_ln_b': (0.0, 0.8),
     'L0_ffn_b1': (0.0, 0.8),
     'L0_ffn_b2': (0.0, 0.1)}
    factors = {'L0_ffn_W1': 3.648, 'L0_ffn_W2': 3.584}
    for name, (base, spread) in spreads.items():
        noise = np.random.default_rng([zlib.crc32(name.encode()), seed]).standard_normal(out[name].shape)
        drawn = base * np.exp(spread * noise) if base else spread * noise
        out[name] = jnp.asarray(drawn.astype(out[name].dtype))
    for name, factor in factors.items():
        out[name] = (out[name] * factor).astype(out[name].dtype)
    return out
```

```python
from contextlib import ExitStack

import concourse.bass as bass
import numpy as np
from concourse import mybir

F32 = mybir.dt.float32
BF16 = mybir.dt.bfloat16
ALU = mybir.AluOpType
ACT = mybir.ActivationFunctionType
AX = mybir.AxisListType

P = 128
BATCH, SEQ = 8, 512
NBLK = SEQ // P
MASKED = -1e30
MASKED1 = -1e28

H1, DH1 = 16, 8
QUAD = 4
NQ = H1 // QUAD
ITERS = 4
SCALE1 = float(1.0 / DH1 ** 0.5)
UNIT = [P * (u + 1) for u in range(NBLK)]
OFF = [sum(UNIT[:u]) for u in range(NBLK)]
ROW = sum(UNIT)
NU = QUAD * NBLK
VW = DH1 + 1
ACT_SQ = [(t, h) for t in range(ITERS) for pair in (0, 1) for h in (2 * pair, 2 * pair + 1)
          if h % 2 == 1]
DVE_SQ = [(t, h) for t in range(ITERS) for pair in (0, 1) for h in (2 * pair, 2 * pair + 1)
          if (t, h) not in ACT_SQ]
PIECES = [(0, 3), (OFF[2], 3), (OFF[3], 4)]
BLOCKS = [[(0, 0), (1, 0), (1, 1)], [(2, k) for k in range(3)], [(3, k) for k in range(4)]]
NPC = len(PIECES)

DEPTH, H2, DH2, WIN = 6, 16, 64, 32
HALF = DH2 // 2
INNER = H2 * DH2
GRP = 4
NG = H2 // GRP
FFN = 341
FCH = [128, 128, FFN - 256]
QK_SCALE = 8.0
LN_SCALE = float(2.0 ** 36)
NWQ = 3 * GRP * DH2
STEPS = DEPTH * BATCH
NVEC = 13
HIST = STEPS + BATCH

C_ID, C_CM, C_WM, C_BO, C_AV, C_RO = 0, 128, 256, 768, 896, 1024
NCONST = C_RO + 4 * SEQ


def stage1(nc, x, consts, w1qk, w1vo, x1d, hist):
    with ExitStack() as ctx:
        def sb(name, shape, dt=F32):
            return ctx.enter_context(nc.sbuf_tensor(name, shape, dt))

        def ps(name, shape):
            return ctx.enter_context(nc.psum_tensor(name, shape, F32))

        def sem(name):
            return ctx.enter_context(nc.semaphore(name))

        ident = sb("ident", [P, P])
        cmask = sb("cmask", [P, P])
        identb = sb("identb", [P, P], BF16)
        cmaskb = sb("cmaskb", [P, P], BF16)
        wqk = sb("wqk", [P, 2, NQ, P])
        wvo = sb("wvo", [P, 2, P])
        xin = sb("xin", [P, NBLK, P])
        xres = sb("xres", [P, NBLK, P])
        x1 = sb("x1", [P, NBLK, P])
        hin = sb("hin", [P, NBLK, P])
        hout = sb("hout", [P, NBLK, P])
        hT = sb("hT", [P, SEQ])
        houtT = sb("houtT", [P, SEQ])
        qT = sb("qT", [P, NQ, SEQ])
        kT = sb("kT", [P, NQ, SEQ])
        vals = sb("vals", [P, NBLK, H1, VW])
        S = sb("S", [P, 2, QUAD, ROW])
        R = sb("R", [P, QUAD, ROW])
        W = sb("W", [P, QUAD, ROW])
        WT = sb("WT", [P, 2, SEQ])
        attn = sb("attn", [P, NBLK, P])
        attnT = sb("attnT", [P, SEQ])
        rden = sb("rden", [P, NBLK, QUAD])
        smax = sb("smax", [P, 2, NU])
        lam = sb("lam", [P, 2, NU])
        sum1 = sb("sum1", [P, NU])
        sum2 = sb("sum2", [P, NU])
        step = sb("step", [P, 2, NU])
        stat = [sb(f"stat{i}", [P, NBLK, 6]) for i in range(2)]
        mv = [sb(f"mv{i}", [P, NBLK, 2]) for i in range(2)]
        var = [sb(f"var{i}", [P, 3, NBLK]) for i in range(2)]
        zero = sb("zero", [P, 1])

        psS = ps("psS", [P, NBLK, SEQ])
        psT = ps("psT", [P, 2, SEQ])
        psO = ps("psO", [P, SEQ])
        psM = ps("psM", [P, SEQ])

        const_in = sem("const_in")
        masks = sem("masks")
        cleared = sem("cleared")
        xin_in = sem("xin_in")
        xres_in = sem("xres_in")
        x1_out = sem("x1_out")
        hist_out = sem("hist_out")
        s_score = sem("s_score")
        s_evac = sem("s_evac")
        s_lam0 = sem("s_lam0")
        s_root = sem("s_root")
        s_asq = sem("s_asq")
        s_dsq = sem("s_dsq")
        s_sq2 = sem("s_sq2")
        s_step = sem("s_step")
        s_lam = sem("s_lam")
        s_w = sem("s_w")
        s_tr = sem("s_tr")
        s_trev = sem("s_trev")
        s_pv = sem("s_pv")
        s_quad = sem("s_quad")
        s_rden = sem("s_rden")
        s_attn = sem("s_attn")
        s_m = sem("s_m")
        s_mev = sem("s_mev")
        s_x1 = sem("s_x1")
        s_ln = [sem("s_ln_in"), sem("s_ln_out")]
        s_rs = [sem("s_rs_in"), sem("s_rs_out")]

        M_PRO, M_B = 9, 13
        E_PRO, E_B = 9, 12
        LN = 8

        block = ctx.enter_context(nc.Block())

        @block.sync
        def _(sp):
            sp.dma_start(ident[:, :], consts[:, C_ID:C_ID + P]).then_inc(const_in, 16)
            sp.dma_start(cmask[:, :], consts[:, C_CM:C_CM + P]).then_inc(const_in, 16)
            sp.dma_start(wqk[:, :, :, :], w1qk).then_inc(const_in, 16)
            sp.dma_start(wvo[:, :, :], w1vo).then_inc(const_in, 16)
            sp.dma_start(xin[:, :, :], x[0].rearrange("(k p) d -> p k d", p=P)).then_inc(xin_in, 16)

            def tokens(t, i):
                return t[bass.ds(i, 1)].rearrange("a (k p) d -> p (a k) d", p=P)

            def store(b):
                sp.wait_ge(s_x1, b + 1)
                sp.dma_start(tokens(x1d, b - 1), x1[:, :, :]).then_inc(x1_out, 16)
                sp.wait_ge(s_mev, b * E_B + E_PRO + 2)
                sp.dma_start(hist[bass.ds(b - 1, 1)].rearrange("a p n -> (a p) n"), houtT[:, :])\
                  .then_inc(hist_out, 16)

            def sequence(b, last=False):
                first = isinstance(b, int) and b == 0
                if not first:
                    sp.wait_ge(s_x1, b)
                    sp.dma_start(xres[:, :, :], tokens(x, b - 1)).then_inc(xres_in, 16)
                sp.wait_ge(s_ln[0], b * LN + LN)
                if last:
                    sp.sem_inc(xin_in, 16)
                else:
                    sp.dma_start(xin[:, :, :], tokens(x, b + 1)).then_inc(xin_in, 16)
                if not first:
                    store(b)

            sequence(0)
            with sp.Fori(1, BATCH - 1) as b:
                sequence(b)
            sequence(BATCH - 1, last=True)
            sp.wait_ge(s_x1, BATCH)
            sp.dma_start(xres[:, :, :], tokens(x, BATCH - 1)).then_inc(xres_in, 16)
            store(BATCH)
            sp.wait_ge(x1_out, 16 * BATCH + 32)
            sp.wait_ge(hist_out, 16 * BATCH + 32)

        @block.tensor
        def _(pe):
            def m_free(n_ev):
                pe.wait_ge(s_mev, n_ev)

            def turn_h(base):
                pe.wait_ge(s_ln[0], base[1])
                m_free(base[0])
                for k in range(NBLK):
                    mm = pe.transpose(psM[:, k * P:(k + 1) * P], hin[:, k, :], ident[:, :])
                mm.then_inc(s_m, 1)

            def project(which, j, n_ev):
                m_free(n_ev)
                pe.matmul(psM[:, :], wqk[:, which, j, :], hT[:, :], start=True, stop=True).then_inc(s_m, 1)

            def scores(N, j, h):
                for u in range(NBLK):
                    pe.wait_ge(s_evac, N * NU + h * NBLK + u + 1)
                    pe.matmul(psS[:, u, 0:UNIT[u]], qT[32 * h:32 * h + DH1, j, u * P:(u + 1) * P],
                              kT[32 * h:32 * h + DH1, j, 0:UNIT[u]], start=True, stop=True)
                    pe.matmul(psS[:, u, u * P:UNIT[u]], identb[:, :], cmaskb[:, :],
                              start=False, stop=True, skip_group_check=True).then_inc(s_score, 1)

            def turn(N, h, i):
                t = N * QUAD * NPC + h * NPC + i
                if i == 0:
                    pe.wait_ge(s_w, N * QUAD + h + 1)
                pe.wait_ge(s_trev, t + 1)
                c, n = PIECES[i]
                for m in range(n):
                    mm = pe.transpose(psT[:, (h * NPC + i) % 2, m * P:(m + 1) * P],
                                      W[:, h, c + m * P:c + (m + 1) * P], ident[:, :])
                mm.then_inc(s_tr, 1)

            def weigh(N, jprev, h, i):
                t = N * QUAD * NPC + h * NPC + i
                pe.wait_ge(s_trev, t + 3)
                if h == 0 and i == 0:
                    pe.wait_ge(s_attn, N + 1)
                for m, (u, k) in enumerate(BLOCKS[i]):
                    head = jprev * QUAD + h
                    o = (u * QUAD + h) * VW
                    mm = pe.matmul(psO[:, o:o + VW], WT[:, (h * NPC + i) % 2, m * P:(m + 1) * P],
                                   vals[:, k, head, :], start=(k == 0), stop=(k == u))
                mm.then_inc(s_pv, 1)

            def head_out(N, jprev, h):
                for i in range(NPC):
                    turn(N, h, i)
                    if i:
                        weigh(N, jprev, h, i - 1)
                weigh(N, jprev, h, NPC - 1)

            def turn_attn(b):
                pe.wait_ge(s_attn, b * NQ + 2)
                m_free(b * E_B + E_PRO)
                for k in range(NBLK):
                    mm = pe.transpose(psM[:, k * P:(k + 1) * P], attn[:, k, :], ident[:, :])
                mm.then_inc(s_m, 1)

            def out_project(b):
                m_free(b * E_B + E_PRO + 1)
                for k in range(NBLK):
                    mm = pe.matmul(psM[:, k * P:(k + 1) * P], attnT[:, k * P:(k + 1) * P], wvo[:, 1, :],
                                   start=True, stop=True)
                mm.then_inc(s_m, 1)

            def turn_out(b):
                pe.wait_ge(s_ln[1], b * LN + LN)
                for k in range(NBLK):
                    mm = pe.transpose(psM[:, k * P:(k + 1) * P], hout[:, k, :], ident[:, :])
                mm.then_inc(s_m, 1)

            def values(b):
                m_free(b * E_B + E_PRO + 2)
                for k in range(NBLK):
                    mm = pe.matmul(psM[:, k * P:(k + 1) * P], hT[:, k * P:(k + 1) * P], wvo[:, 0, :],
                                   start=True, stop=True)
                mm.then_inc(s_m, 1)

            pe.wait_ge(const_in, 64)
            pe.wait_ge(masks, 2)
            pe.wait_ge(cleared, 1)
            pe.wait_ge(s_ln[0], LN)
            for k in range(NBLK):
                mm = pe.transpose(psM[:, k * P:(k + 1) * P], hin[:, k, :], ident[:, :])
            mm.then_inc(s_m, 1)
            for j in range(NQ):
                project(0, j, 1 + 2 * j)
                project(1, j, 2 + 2 * j)
            pe.wait_ge(s_mev, E_PRO)
            for h in range(QUAD):
                scores(0, 0, h)

            with pe.Fori(0, BATCH) as b:
                for j in range(NQ):
                    N = b * NQ + j
                    nxt, prev = (j + 1) % NQ, (j - 1) % NQ
                    e = b * E_B + E_PRO
                    scores(N + 1, nxt, 0)
                    if j == 1:
                        pe.wait_ge(s_mev, e + 3)
                    head_out(N, prev, 0)
                    head_out(N, prev, 1)
                    scores(N + 1, nxt, 1)
                    head_out(N, prev, 2)
                    head_out(N, prev, 3)
                    scores(N + 1, nxt, 2)
                    if j == 0:
                        turn_attn(b)
                        out_project(b)
                    if j == 2:
                        turn_h((e + 3, b * LN + 2 * LN))
                    if j == 3:
                        project(0, 1, e + 6)
                        project(1, 1, e + 7)
                    scores(N + 1, nxt, 3)
                    if j == 0:
                        turn_out(b)
                        values(b)
                    if j == 2:
                        project(0, 0, e + 4)
                        project(1, 0, e + 5)
                        pe.wait_ge(s_mev, e + 6)
                    if j == 3:
                        for g in (2, 3):
                            project(0, g, e + 4 + 2 * g)
                            project(1, g, e + 5 + 2 * g)
                        pe.wait_ge(s_mev, e + 12)
            for h in range(QUAD):
                head_out(BATCH * NQ, NQ - 1, h)
            turn_attn(BATCH)
            out_project(BATCH)
            turn_out(BATCH)

        @block.scalar
        def _(act):
            def evac(dst, n):
                act.wait_ge(s_m, n)
                nc.scalar.copy(dst, psM[:, :]).then_inc(s_mev, 1)

            def evac_values(n):
                act.wait_ge(s_m, n)
                nc.scalar.copy(vals[:, :, :, 0:DH1], psM[:, :].rearrange("p (k h d) -> p k h d", k=NBLK, h=H1))\
                    .then_inc(s_mev, 1)

            def evac_out(b):
                act.wait_ge(hist_out, b * 16 + 16)
                evac(houtT[:, :], b * M_B + M_PRO + 3)

            def rstd(which, n):
                act.wait_ge(s_ln[which], n)
                nc.scalar.activation(var[which][:, 1, :], var[which][:, 0, :], ACT.Abs_reciprocal_sqrt,
                                     bias=zero[:, 0:1]).then_inc(s_rs[which], 1)

            def pieces(N, h):
                for i in range(NPC):
                    t = N * QUAD * NPC + h * NPC + i
                    n = PIECES[i][1] * P
                    act.wait_ge(s_tr, t + 1)
                    act.wait_ge(s_pv, t + 1)
                    nc.scalar.copy(WT[:, (h * NPC + i) % 2, 0:n], psT[:, (h * NPC + i) % 2, 0:n])\
                        .then_inc(s_trev, 1)

            act.wait_ge(cleared, 1)
            act.wait_ge(masks, 2)
            rstd(0, 3)
            evac(hT[:, :], 1)
            for j in range(NQ):
                evac(qT[:, j, :], 2 + 2 * j)
                evac(kT[:, j, :], 3 + 2 * j)

            with act.Fori(0, BATCH) as b:
                for j in range(NQ):
                    N = b * NQ + j
                    par = j % 2
                    m = b * M_B + M_PRO
                    for t in range(ITERS + 1):
                        for pair in (0, 1):
                            if t:
                                act.wait_ge(s_lam, N * 2 * ITERS + 2 * (t - 1) + pair + 1)
                            elif pair == 0:
                                act.wait_ge(s_lam0, N + 1)
                            for h in (2 * pair, 2 * pair + 1):
                                if t == 0:
                                    act.wait_ge(s_w, N * QUAD + h + 1)
                                for u in range(NBLK):
                                    c = slice(OFF[u], OFF[u] + UNIT[u])
                                    i = h * NBLK + u
                                    nc.scalar.activation(R[:, h, c], S[:, par, h, c], ACT.Abs_reciprocal_sqrt,
                                                         bias=lam[:, par, i:i + 1], scale=-1.0).then_inc(s_root, 1)
                            for h in (2 * pair, 2 * pair + 1):
                                if (t, h) in ACT_SQ:
                                    for u in range(NBLK):
                                        c = slice(OFF[u], OFF[u] + UNIT[u])
                                        i = h * NBLK + u
                                        act.wait_ge(s_root, ((N * (ITERS + 1) + t) * NU) + i + 1)
                                        nc.scalar.activation(R[:, h, c], R[:, h, c], ACT.Square,
                                                             accum_out=sum1[:, i:i + 1]).then_inc(s_asq, 1)
                            if j == 1 and (t, pair) == (0, 0):
                                evac_values(m + 4)
                            if t < 2:
                                pieces(N, 2 * t + pair)
                            if j == 0 and (t, pair) == (2, 1):
                                evac(attnT[:, :], m + 1)
                            if j == 0 and (t, pair) == (3, 1):
                                rstd(1, b * LN + 3)
                            if j == 0 and (t, pair) == (4, 1):
                                evac_out(b)
                            if j == 2 and (t, pair) == (0, 1):
                                rstd(0, b * LN + LN + 3)
                            if j == 2 and (t, pair) == (3, 0):
                                evac(hT[:, :], m + 5)
                            if j == 2 and t == 4:
                                evac((qT, kT)[pair][:, 0, :], m + 6 + pair)
                            if j == 3 and (t == 2 or (t, pair) in ((3, 1), (4, 0))):
                                i = {(2, 0): 0, (2, 1): 1, (3, 1): 2, (4, 0): 3}[(t, pair)]
                                evac((qT, kT)[i % 2][:, 1 + i // 2, :], m + 8 + i)
                            if j == 3 and (t, pair) == (4, 1):
                                evac(qT[:, 3, :], m + 12)
                                evac(kT[:, 3, :], m + 13)
            for h in range(QUAD):
                pieces(BATCH * NQ, h)
            m = BATCH * M_B + M_PRO
            evac(attnT[:, :], m + 1)
            rstd(1, BATCH * LN + 3)
            evac_out(BATCH)

        @block.gpsimd
        def _(pool):
            nc.gpsimd.memset(W[:, :, :], 1.0)
            nc.gpsimd.memset(vals[:, :, :, :], 1.0)
            nc.gpsimd.memset(xres[:, :, :], 1.0)
            nc.gpsimd.memset(zero[:, :], 0.0).then_inc(cleared, 1)
            pool.wait_ge(cleared, 1)
            pool.sem_inc(s_w, QUAD)
            pool.sem_inc(xres_in, 16)
            pool.sem_inc(x1_out, 32)
            pool.sem_inc(hist_out, 32)
            pool.sem_inc(s_evac, NBLK)
            pool.sem_inc(s_trev, 2)
            pool.sem_inc(s_pv, 2)
            pool.sem_inc(s_attn, 1)
            with pool.Fori(0, BATCH * NQ) as N:
                for h in range(QUAD):
                    pool.wait_ge(s_root, (N * (ITERS + 1) + ITERS) * NU + (h + 1) * NBLK)
                    pool.wait_ge(s_tr, N * QUAD * NPC + (h + 1) * NPC)
                    nc.gpsimd.tensor_tensor(W[:, h, :], R[:, h, :], R[:, h, :], ALU.mult).then_inc(s_w, 1)

        @block.vector
        def _(dve):
            def ln_stats(which, src, n):
                s = s_ln[which]
                for k in range(NBLK):
                    ins = nc.vector.bn_stats(out=stat[which][:, k, :], in_=src[:, k, :])
                ins.then_inc(s, 1)
                dve.wait_ge(s, n + 1)
                nc.vector.memset(var[which][:, 1, :], 1.0)
                for k in range(NBLK):
                    ins = nc.vector.bn_aggr(out=mv[which][:, k, :], in_=stat[which][:, k, :])
                ins.then_inc(s, 1)
                dve.wait_ge(s, n + 2)
                nc.vector.tensor_scalar(var[which][:, 0, :], mv[which][:, :, 1], 1e-5, None, ALU.add).then_inc(s, 1)

            def ln_apply(which, src, dst, n, nrs):
                s = s_ln[which]
                v, y, t = (var[which][:, i, :] for i in range(3))
                dve.wait_ge(s_rs[which], nrs)
                nc.vector.tensor_tensor(t, y, y, ALU.mult).then_inc(s, 1)
                dve.wait_ge(s, n + 4)
                nc.vector.tensor_tensor(t, t, v, ALU.mult).then_inc(s, 1)
                dve.wait_ge(s, n + 5)
                nc.vector.tensor_scalar(t, t, -0.5, 1.5, ALU.mult, ALU.add).then_inc(s, 1)
                dve.wait_ge(s, n + 6)
                nc.vector.tensor_tensor(y, y, t, ALU.mult).then_inc(s, 1)
                dve.wait_ge(s, n + 7)
                for k in range(NBLK):
                    ins = nc.vector.tensor_scalar(dst[:, k, :], src[:, k, :], mv[which][:, k, 0:1],
                                                  var[which][:, 1, k:k + 1], ALU.subtract, ALU.mult)
                ins.then_inc(s, 1)

            def scores_in(N, par, h):
                for u in range(NBLK):
                    c = slice(OFF[u], OFF[u] + UNIT[u])
                    i = h * NBLK + u
                    dve.wait_ge(s_score, N * NU + i + 1)
                    nc.vector.tensor_scalar(S[:, par, h, c], psS[:, u, 0:UNIT[u]], SCALE1, None, ALU.mult,
                                            ALU.max, accum_out=smax[:, par, i:i + 1]).then_inc(s_evac, 1)

            def first_lam(N, par):
                dve.wait_ge(s_evac, N * NU + NU + NBLK)
                nc.vector.tensor_scalar(lam[:, par, :], smax[:, par, :], 1.0, None, ALU.add).then_inc(s_lam0, 1)

            def newton(N, par, t, pair):
                heads = (2 * pair, 2 * pair + 1)
                for h in heads:
                    if (t, h) in DVE_SQ:
                        for u in range(NBLK):
                            c = slice(OFF[u], OFF[u] + UNIT[u])
                            i = h * NBLK + u
                            dve.wait_ge(s_root, (N * (ITERS + 1) + t) * NU + i + 1)
                            nc.vector.tensor_tensor_reduce(out=R[:, h, c], in0=R[:, h, c], in1=R[:, h, c], scale=1.0,
                                                           scalar=0.0, op0=ALU.mult, op1=ALU.add,
                                                           accum_out=sum1[:, i:i + 1]).then_inc(s_dsq, 1)
                for h in heads:
                    for u in range(NBLK):
                        c = slice(OFF[u], OFF[u] + UNIT[u])
                        i = h * NBLK + u
                        if (t, h) in DVE_SQ:
                            dve.wait_ge(s_dsq, (N * len(DVE_SQ) + DVE_SQ.index((t, h))) * NBLK + u + 1)
                        else:
                            dve.wait_ge(s_asq, (N * len(ACT_SQ) + ACT_SQ.index((t, h))) * NBLK + u + 1)
                        nc.vector.tensor_tensor_reduce(out=R[:, h, c], in0=R[:, h, c], in1=R[:, h, c], scale=1.0,
                                                       scalar=0.0, op0=ALU.mult, op1=ALU.add,
                                                       accum_out=sum2[:, i:i + 1]).then_inc(s_sq2, 1)
                n = N * 2 * ITERS + 2 * t + pair
                c = slice(2 * pair * NBLK, 2 * (pair + 1) * NBLK)
                dve.wait_ge(s_sq2, (n + 1) * 2 * NBLK)
                nc.vector.reciprocal(step[:, 0, c], sum2[:, c]).then_inc(s_step, 1)
                dve.wait_ge(s_step, n * 2 + 1)
                nc.vector.scalar_tensor_tensor(out=step[:, 1, c], in0=sum1[:, c], scalar=-1.0, in1=step[:, 0, c],
                                               op0=ALU.add, op1=ALU.mult).then_inc(s_step, 1)
                dve.wait_ge(s_step, n * 2 + 2)
                nc.vector.tensor_tensor(lam[:, par, c], lam[:, par, c], step[:, 1, c], ALU.add).then_inc(s_lam, 1)

            def quad_out(N, jprev):
                o = psO[:, 0:NBLK * QUAD * VW].rearrange("p (u h v) -> p u h v", u=NBLK, h=QUAD)
                dve.wait_ge(s_pv, N * QUAD * NPC + QUAD * NPC + 2)
                nc.vector.reciprocal(rden[:, :, :], o[:, :, :, DH1]).then_inc(s_rden, 1)
                dve.wait_ge(s_rden, N + 1)
                a = attn[:, :, jprev * QUAD * DH1:(jprev + 1) * QUAD * DH1].rearrange("p u (h d) -> p u h d", h=QUAD)
                nc.vector.tensor_tensor(a, o[:, :, :, 0:DH1],
                                        rden[:, :, :].unsqueeze(3).broadcast_to([P, NBLK, QUAD, DH1]),
                                        ALU.mult).then_inc(s_attn, 1)

            def residual(b):
                dve.wait_ge(s_m, b * M_B + M_PRO + 2)
                dve.wait_ge(xres_in, b * 16 + 16)
                dve.wait_ge(x1_out, b * 16 + 16)
                nc.vector.tensor_tensor(x1[:, :, :], psM[:, :].rearrange("p (k d) -> p k d", k=NBLK),
                                        xres[:, :, :], ALU.add).then_inc(s_x1, 1)
                dve.wait_ge(s_x1, b + 1)

            nc.vector.memset(attn[:, :, :], 0.0)
            dve.wait_ge(const_in, 64)
            nc.vector.tensor_copy(identb[:, :], ident[:, :]).then_inc(masks, 1)
            nc.vector.tensor_copy(cmaskb[:, :], cmask[:, :]).then_inc(masks, 1)
            dve.wait_ge(masks, 2)
            dve.wait_ge(xin_in, 16)
            ln_stats(0, xin, 0)
            ln_apply(0, xin, hin, 0, 1)
            for h in range(QUAD):
                scores_in(0, 0, h)
            first_lam(0, 0)

            with dve.Fori(0, BATCH) as b:
                for j in range(NQ):
                    N = b * NQ + j
                    par = j % 2
                    for t in range(ITERS):
                        if t == 2:
                            quad_out(N, (j - 1) % NQ)
                        newton(N, par, t, 0)
                        if j == 0 and t == 3:
                            residual(b)
                            ln_stats(1, x1, b * LN)
                        if j == 2 and t == 0:
                            dve.wait_ge(xin_in, b * 16 + 32)
                            ln_stats(0, xin, b * LN + LN)
                        newton(N, par, t, 1)
                        scores_in(N + 1, 1 - par, t)
                        if j == 2 and t == 1:
                            ln_apply(0, xin, hin, b * LN + LN, b + 2)
                    first_lam(N + 1, 1 - par)
                    if j == 0:
                        ln_apply(1, x1, hout, b * LN, b + 1)
            quad_out(BATCH * NQ, NQ - 1)
            residual(BATCH)
            ln_stats(1, x1, BATCH * LN)
            ln_apply(1, x1, hout, BATCH * LN, BATCH + 1)


def stage2(nc, consts, wqkv, wod, w1d, w2d, vecd, hist):
    with ExitStack() as ctx:
        def sb(name, shape, dt=F32):
            return ctx.enter_context(nc.sbuf_tensor(name, shape, dt))

        def ps(name, shape):
            return ctx.enter_context(nc.psum_tensor(name, shape, F32))

        def sem(name):
            return ctx.enter_context(nc.semaphore(name))

        wg = sb("wg", [P, NG, NWQ])
        wo = sb("wo", [P, INNER // P, P])
        w1 = sb("w1", [P, 2 * FFN])
        w2 = sb("w2", [P, 3, P])
        vec = sb("vec", [P, NVEC])
        vecq = sb("vecq", [P, 4])
        ident = sb("ident2", [P, P])
        wmask = sb("wmask", [P, SEQ])
        ones4 = sb("ones4", [P, P])
        avg = sb("avg", [P, P])
        rope = sb("rope", [P, 4, SEQ])
        tab = sb("tab", [P, 2, 2, 2, SEQ])
        xs = sb("xs", [P, SEQ + 1])
        xr = sb("xr", [P, SEQ])
        xm = sb("xm", [P, SEQ + 1])
        sq = sb("sq", [P, 2, 2, SEQ])
        sqs = sb("sqs", [P, 2, SEQ])
        m1 = sb("m1", [P, 2, 2, SEQ])
        m2 = sb("m2", [P, 2, 2, SEQ])
        lnn = sb("lnn", [P, 2, SEQ])
        rn = sb("rn", [P, 2, SEQ])
        nf = sb("nf", [P, 2, 2, SEQ])
        qkn = sb("qkn", [P, 2, 2, 2, WIN + SEQ])
        sm = sb("sm", [P, 2, SEQ])
        pr = sb("pr", [P, 2, 2, SEQ])
        mx = sb("mx", [P, 16])
        sums = sb("sums", [P, 16])
        rsum = sb("rsum", [P, 16])
        pT = sb("pT", [P, 2, SEQ])
        v = sb("v", [P, NBLK, INNER])
        vr = sb("vr", [P, NBLK, INNER])
        oT = sb("oT", [P, INNER // P, SEQ])
        xc = sb("xc", [P, SEQ])
        xc2 = sb("xc2", [P, SEQ])
        lnv = sb("lnv", [P, SEQ])
        rstd = sb("rstd", [P, SEQ])
        xn = sb("xn", [P, SEQ])
        gl = sb("gl", [P, 3, SEQ])
        xo = sb("xo", [P, SEQ])
        cst = sb("cst", [P, 4])

        pj = [ps(f"pj{i}", [P, 2, SEQ]) for i in range(2)]
        gp = [ps(f"gp{i}", [P, 2, SEQ]) for i in range(2)]

        const_in = sem("const_in2")
        cleared = sem("cleared2")
        wg_in = [sem(f"wg_in{g}") for g in range(NG)]
        late_in = sem("late_in")
        vecq_in = sem("vecq_in")
        xs_in = sem("xs_in")
        xr_in = sem("xr_in")
        x_out = sem("x_out")
        q_in = [sem("q_in0"), sem("q_in1")]
        vr_in = [sem("vr_in0"), sem("vr_in1")]
        s_tab = sem("s_tab")
        s_proj = sem("s_proj")
        s_sq = sem("s_sq")
        s_rot = sem("s_rot")
        s_sqs = sem("s_sqs")
        s_add = sem("s_add")
        s_norm = sem("s_norm")
        s_lnn = sem("s_lnn")
        s_rn = sem("s_rn")
        s_nf = sem("s_nf")
        s_sc = sem("s_sc")
        s_mask = sem("s_mask")
        s_max = sem("s_max")
        s_sub = sem("s_sub")
        s_exp = sem("s_exp")
        s_sum = sem("s_sum")
        s_rsum = sem("s_rsum")
        s_pr = sem("s_pr")
        s_pT = sem("s_pT")
        s_pTev = sem("s_pTev")
        s_pv = sem("s_pv2")
        s_oT = sem("s_oT")
        s_v = sem("s_v")
        s_vev = sem("s_vev")
        s_wo = sem("s_wo")
        s_xm = sem("s_xm")
        s_mean = sem("s_mean")
        s_xc = sem("s_xc")
        s_xc2 = sem("s_xc2")
        s_var = sem("s_var")
        s_lnv = sem("s_lnv")
        s_rstd = sem("s_rstd")
        s_xcr = sem("s_xcr")
        s_xn = sem("s_xn")
        s_w1 = sem("s_w1")
        s_gl = sem("s_gl")
        s_ug = sem("s_ug")
        s_w2 = sem("s_w2")
        s_xo = sem("s_xo")
        held = {e: sem(f"held_{e}") for e in ("pe", "pool", "dve", "sp")}

        block = ctx.enter_context(nc.Block())

        def slot(t, i):
            return t[bass.ds(i, 1)].rearrange("a p n -> (a p) n")

        EVAC = {"mean": (s_xc, 1, 1), "var": (s_lnv, 1, 1), "wo": (s_xm, 1, 1), "out": (s_xo, 1, 2),
                "gate0": (s_gl, 3, 2), "gate1": (s_gl, 3, 3), "up0": (s_ug, 3, 2), "up1": (s_ug, 3, 3)}
        for g in range(NG):
            EVAC |= {f"score{g}": (s_mask, 4, g + 1), f"norm{g}": (s_lnn, 4, g + 1), f"v{g}": (s_vev, 4, g + 1),
                     f"turn{g}": (s_pTev, 4, g + 1), f"weigh{g}": (s_oT, 8, 2 * g + 4)}
        LOOP = ["turn0", "score0", "norm0", "v0", "weigh0", "v1",
                "turn1", "score1", "norm1", "weigh1", "wo",
                "turn2", "mean", "score2", "norm2", "v2", "v3", "var", "weigh2",
                "turn3", "score3", "norm3", "gate0", "gate1", "up0", "up1", "weigh3", "out"]
        TAIL = ["score0", "turn0", "weigh0", "turn1", "weigh1", "wo", "mean", "var",
                "gate0", "gate1", "up0", "up1", "out"]
        assert len(LOOP) % 2 == 0

        def bank(tasks, name):
            return gp[tasks.index(name) % 2]

        @block.sync
        def _(sp):
            for dst, c in ((ident, C_ID), (wmask, C_WM), (ones4, C_BO), (avg, C_AV)):
                sp.dma_start(dst[:, :], consts[:, c:c + dst.shape[1]]).then_inc(const_in, 16)
            sp.dma_start(rope[:, :, :], consts[:, C_RO:NCONST].rearrange("p (r n) -> p r n", r=4)).then_inc(const_in, 16)
            sp.wait_ge(cleared, 2)

            def load_early(l):
                it = l * BATCH
                sp.wait_ge(s_tab, l * 8 + 8)
                sp.dma_start(vecq[:, :], slot(vecd, l)[:, 9:13]).then_inc(vecq_in, 16)
                for g in range(NG):
                    sp.wait_ge(s_proj, it * 8 + 2 * g + 2)
                    sp.sem_inc(held["sp"], 1)
                    sp.wait_ge(s_v, it * 4 + (2 if g < 2 else 4))
                    sp.dma_start(wg[:, g, :], slot(wqkv, l)[:, g * NWQ:(g + 1) * NWQ]).then_inc(wg_in[g], 16)

            def load_late(it, l):
                sp.wait_ge(s_xo, it + 2)
                sp.dma_start(wo[:, :, :], wod[bass.ds(l, 1)].rearrange("a p c n -> p (a c) n")).then_inc(late_in, 16)
                sp.dma_start(w1[:, :], slot(w1d, l)).then_inc(late_in, 16)
                sp.dma_start(w2[:, :, :], w2d[bass.ds(l, 1)].rearrange("a p c n -> p (a c) n")).then_inc(late_in, 16)
                sp.dma_start(vec[:, :], slot(vecd, l)).then_inc(late_in, 16)

            def rotated(it, g):
                p = g % 2
                sp.wait_ge(s_nf, it * 8 + 2 * g + 3)
                sp.sem_inc(held["sp"], 1)
                sp.wait_ge(s_sc, it * 4 + g + 1)
                for h in range(GRP):
                    hh, b = h // 2, h % 2
                    for half in range(2):
                        r = 64 * b + 32 * half
                        sp.dma_start(qkn[r:r + 32, p, hh, :, WIN:WIN + SEQ], nf[32 * h:32 * h + 32, :, half, :])\
                          .then_inc(q_in[p], 16)

            def rolled(it, half):
                c = slice(half * SEQ, (half + 1) * SEQ)
                sp.wait_ge(s_vev, it * 4 + 2 * half + 2)
                sp.dma_start(vr[0:P - WIN, :, c], v[WIN:P, :, c]).then_inc(vr_in[half], 16)
                sp.dma_start(vr[P - WIN:P, 0:NBLK - 1, c], v[0:WIN, 1:NBLK, c]).then_inc(vr_in[half], 16)
                sp.dma_start(vr[P - WIN:P, NBLK - 1, c], v[0:WIN, 0, c]).then_inc(vr_in[half], 16)

            def load_xs(it, read):
                sp.wait_ge(x_out, it * 16)
                sp.sem_inc(held["sp"], 1)
                sp.wait_ge(s_proj, read)
                sp.sem_inc(held["sp"], 1)
                sp.dma_start(xs[0:64, 0:SEQ], slot(hist, it)[0:64, :]).then_inc(xs_in, 16)
                sp.dma_start(xs[64:P, 1:SEQ], slot(hist, it)[64:P, 0:SEQ - 1]).then_inc(xs_in, 16)

            def step(it, late=None):
                rotated(it, 0)
                rolled(it, 0)
                rotated(it, 1)
                sp.wait_ge(s_xm, it + 1)
                sp.sem_inc(held["sp"], 1)
                sp.dma_start(xr[:, :], slot(hist, it)).then_inc(xr_in, 16)
                rotated(it, 2)
                rolled(it, 1)
                sp.wait_ge(s_v, it * 4 + 8)
                sp.sem_inc(held["sp"], 1)
                load_xs(it + 1, it * 8 + 16)
                rotated(it, 3)
                if not (isinstance(it, int) and it == 0):
                    sp.wait_ge(s_xo, it + 2)
                    sp.dma_start(slot(hist, it + (BATCH - 1)), xo[:, :]).then_inc(x_out, 16)
                if late is not None:
                    load_late(it, late)

            sp.dma_start(xs[0:64, 0:SEQ], hist[0, 0:64, :]).then_inc(xs_in, 16)
            sp.dma_start(xs[64:P, 1:SEQ], hist[0, 64:P, 0:SEQ - 1]).then_inc(xs_in, 16)
            load_early(0)
            step(0, 0)
            with sp.Fori(1, BATCH) as b:
                step(b)
            with sp.Fori(1, DEPTH) as l:
                load_early(l)
                step(l * BATCH, l)
                with sp.Fori(1, BATCH) as b:
                    step(l * BATCH + b)
            sp.wait_ge(s_xo, STEPS + 2)
            sp.dma_start(slot(hist, STEPS + BATCH - 1), xo[:, :]).then_inc(x_out, 16)
            sp.wait_ge(x_out, STEPS * 16 + 32)
            sp.wait_ge(xs_in, STEPS * 32 + 32)

        @block.tensor
        def _(pe):
            def take(tasks, name, it):
                i = tasks.index(name)
                if i >= 2:
                    s, per, k = EVAC[tasks[i - 2]]
                    pe.wait_ge(s, it * per + k)
                else:
                    s, per, k = EVAC[LOOP[i - 2]]
                    pe.wait_ge(s, it * per + k - per)
                return gp[i % 2]

            def project(it, g, which):
                pe.wait_ge(s_rot, it * 8 + 2 * g + which + 1)
                for half in range(2):
                    c = which * 2 * P + half * P
                    mm = pe.matmul(pj[which][:, half, :], wg[:, g, c:c + P], xs[:, 0:SEQ], start=True, stop=True)
                mm.then_inc(s_proj, 1)

            def norms(it, g, out):
                for which in range(2):
                    pe.wait_ge(s_sqs, it * 8 + 2 * g + which + 3)
                    mm = pe.matmul(out[:, which, :], ones4[:, :], sqs[:, which, :], start=True, stop=True)
                mm.then_inc(s_norm, 1)

            def scores(it, g, out):
                p = (g - 1) % 2
                pe.wait_ge(q_in[p], it * 256 + 128 * (g // 2 + 1))
                pe.sem_inc(held["pe"], 1)
                for k in range(NBLK):
                    for s in range(2):
                        for par in range(2):
                            w = (4 * k + 1 + 2 * s + par) % (SEQ // WIN)
                            for hh in range(2):
                                for b in range(2):
                                    o = 32 * (2 * hh + par)
                                    mm = pe.matmul(out[o:o + 32, b, (2 * k + s) * 64:(2 * k + s + 1) * 64],
                                                   qkn[64 * b:64 * b + 64, p, hh, 0, (w + 1) * WIN:(w + 2) * WIN],
                                                   qkn[64 * b:64 * b + 64, p, hh, 1, w * WIN:(w + 2) * WIN],
                                                   start=True, stop=True, tile_position=(64 * b, o))
                mm.then_inc(s_sc, 1)

            def turn(it, g, out):
                pe.wait_ge(s_pr, it * 4 + g + 1)
                for b in range(2):
                    for k in range(NBLK):
                        mm = pe.transpose(out[:, b, k * P:(k + 1) * P], pr[:, g % 2, b, k * P:(k + 1) * P], ident[:, :])
                mm.then_inc(s_pT, 1)

            def weigh(it, g, out):
                pe.wait_ge(s_pTev, it * 4 + g + 1)
                if g % 2 == 0:
                    half = (g + 2) % 4 // 2
                    pe.wait_ge(vr_in[half], it * 48 + (48 if half else 96))
                pe.sem_inc(held["pe"], 1)
                for k in range(NBLK):
                    for par in range(2):
                        src = vr if par else v
                        for hh in range(2):
                            for s in range(2):
                                for b in range(2):
                                    c = (GRP * ((g - 2) % NG) + 2 * hh + b) * DH2
                                    o = (hh * 8 + k * 2 + par) * WIN
                                    r = k * P + (2 * hh + par) * WIN
                                    mm = pe.matmul(out[64 * b:64 * b + 64, s, o:o + WIN],
                                                   src[64 * s:64 * s + 64, k, c:c + DH2],
                                                   pT[64 * s:64 * s + 64, b, r:r + WIN],
                                                   start=True, stop=True, tile_position=(64 * s, 64 * b))
                mm.then_inc(s_pv, 1)

            def values(half, part, out):
                for i in range(2):
                    k = 2 * part + i
                    mm = pe.matmul(out[:, i, :], xs[:, k * P:(k + 1) * P],
                                   wg[:, 2 * half:2 * half + 2, 4 * P:6 * P], start=True, stop=True)
                mm.then_inc(s_v, 1)

            def out_project(it, out):
                pe.wait_ge(s_oT, it * 8 + 6)
                for c in range(INNER // P):
                    mm = pe.matmul(out[:, 0, :], wo[:, c, :], oT[:, c, :], start=(c == 0), stop=(c == INNER // P - 1))
                mm.then_inc(s_wo, 1)

            def average(src, ready, n, out, done):
                pe.wait_ge(ready, n)
                pe.matmul(out[:, 0, :], avg[:, :], src, start=True, stop=True).then_inc(done, 1)

            def hidden(first, chunks, out):
                for i, c in enumerate(chunks):
                    mm = pe.matmul(out[0:FCH[c], i, :], w1[:, first + c * P:first + c * P + FCH[c]], xn[:, :],
                                   start=True, stop=True)
                mm.then_inc(s_w1, 1)

            def ffn(it, tasks):
                pe.wait_ge(s_xn, it + 1)
                for name, first, chunks in (("gate0", FFN, (0, 1)), ("gate1", FFN, (2,)), ("up0", 0, (0, 1)), ("up1", 0, (2,))):
                    hidden(first, chunks, take(tasks, name, it))

            def ffn_out(it, out):
                pe.wait_ge(s_ug, it * 3 + 3)
                for c, n in enumerate(FCH):
                    mm = pe.matmul(out[:, 0, :], w2[0:n, c, :], gl[0:n, c, :], start=(c == 0), stop=(c == 2))
                mm.then_inc(s_w2, 1)

            def step(it, l):
                for g in range(NG):
                    pe.wait_ge(wg_in[g], l * 16 + 16)
                    if g % 2 == 0:
                        pe.wait_ge(wg_in[g + 1], l * 16 + 16)
                    if g == 0:
                        pe.wait_ge(xs_in, it * 32 + 32)
                    project(it, g, 0)
                    project(it, g, 1)
                    turn(it, g, take(LOOP, f"turn{g}", it))
                    if g == 2:
                        average(xm[:, 0:SEQ], s_xm, it + 1, take(LOOP, "mean", it), s_mean)
                    scores(it, g, take(LOOP, f"score{g}", it))
                    norms(it, g, take(LOOP, f"norm{g}", it))
                    if g == 0:
                        values(0, 0, take(LOOP, "v0", it))
                    if g == 2:
                        values(1, 0, take(LOOP, "v2", it))
                        values(1, 1, take(LOOP, "v3", it))
                        average(xc2[:, :], s_xc2, it + 1, take(LOOP, "var", it), s_var)
                    if g == 3:
                        ffn(it, LOOP)
                    weigh(it, g, take(LOOP, f"weigh{g}", it))
                    if g == 0:
                        values(0, 1, take(LOOP, "v1", it))
                    if g == 1:
                        out_project(it, take(LOOP, "wo", it))
                ffn_out(it, take(LOOP, "out", it))
                pe.wait_ge(late_in, l * 64 + 64)

            pe.wait_ge(const_in, 80)
            pe.wait_ge(cleared, 2)
            with pe.Fori(0, DEPTH) as l:
                with pe.Fori(0, BATCH) as b:
                    step(l * BATCH + b, l)
            it = STEPS
            scores(it, 0, take(TAIL, "score0", it))
            for g in range(2):
                turn(it, g, take(TAIL, f"turn{g}", it))
                weigh(it, g, take(TAIL, f"weigh{g}", it))
            out_project(it, take(TAIL, "wo", it))
            average(xm[:, 0:SEQ], s_xm, it + 1, take(TAIL, "mean", it), s_mean)
            average(xc2[:, :], s_xc2, it + 1, take(TAIL, "var", it), s_var)
            ffn(it, TAIL)
            ffn_out(it, take(TAIL, "out", it))

        @block.scalar
        def _(act):
            def squares(it, g, which):
                act.wait_ge(s_proj, it * 8 + 2 * g + which + 9)
                act.wait_ge(s_sqs, it * 8 + 2 * g + which + 1)
                nc.scalar.activation(sq[:, which, :, :], pj[which][:, :, :], ACT.Square).then_inc(s_sq, 1)

            def inverse_norms(it, g):
                act.wait_ge(s_norm, it * 4 + g + 2)
                nc.scalar.activation(lnn[:, :, :], bank(LOOP, f"norm{g}")[:, :, :], ACT.Ln, scale=LN_SCALE,
                                     bias=cst[:, 0:1]).then_inc(s_lnn, 1)
                act.wait_ge(s_lnn, it * 4 + g + 1)
                act.wait_ge(s_nf, it * 8 + 2 * g + 1)
                nc.scalar.activation(rn[:, :, :], lnn[:, :, :], ACT.Exp, scale=-0.5, bias=cst[:, 2:3]).then_inc(s_rn, 1)

            def values(it, n):
                half, part = n // 2, n % 2
                act.wait_ge(s_v, it * 4 + n + 5)
                act.wait_ge(vr_in[half], it * 48 + 48)
                nc.scalar.copy(v[:, 2 * part:2 * part + 2, half * SEQ:(half + 1) * SEQ], bank(LOOP, f"v{n}")[:, :, :])\
                    .then_inc(s_vev, 1)

            def exponentials(it, g):
                act.wait_ge(s_sub, it * 4 + g + 1)
                act.wait_ge(s_pT, it * 4 + g + 1)
                nc.scalar.activation(pr[:, (g - 1) % 2, :, :], sm[:, :, :], ACT.Exp, scale=QK_SCALE).then_inc(s_exp, 1)

            def turned(it, g, tasks):
                act.wait_ge(s_pT, it * 4 + g + 2)
                act.wait_ge(s_pv, it * 4 + g + 1)
                nc.scalar.copy(pT[:, :, :], bank(tasks, f"turn{g}")[:, :, :]).then_inc(s_pTev, 1)

            def squared_deviation(it):
                act.wait_ge(s_xc, it + 1)
                nc.scalar.activation(xc2[:, :], xc[:, :], ACT.Square).then_inc(s_xc2, 1)

            def inverse_deviation(it, tasks):
                act.wait_ge(s_var, it + 1)
                nc.scalar.activation(lnv[:, :], bank(tasks, "var")[:, 0, :], ACT.Ln, bias=cst[:, 1:2]).then_inc(s_lnv, 1)
                act.wait_ge(s_lnv, it + 1)
                nc.scalar.activation(rstd[:, :], lnv[:, :], ACT.Exp, scale=-0.5).then_inc(s_rstd, 1)

            def gelu(it, tasks):
                for c, n in enumerate(FCH):
                    act.wait_ge(s_w1, it * 4 + 1 + c // 2)
                    act.wait_ge(s_w2, it + 1)
                    nc.scalar.activation(gl[0:n, c, :], bank(tasks, f"gate{c // 2}")[0:n, c % 2, :], ACT.Gelu,
                                         bias=vec[0:n, 6 + c:7 + c]).then_inc(s_gl, 1)

            act.wait_ge(cleared, 2)
            with act.Fori(0, DEPTH) as l:
                with act.Fori(0, BATCH) as b:
                    it = l * BATCH + b
                    nc.scalar.preload_act_table_set("natural_log_exp_and_others")
                    for g in range(NG):
                        squares(it, g, 0)
                        squares(it, g, 1)
                        turned(it, g, LOOP)
                        if g == 2:
                            squared_deviation(it)
                        inverse_norms(it, g)
                        if g % 2 == 0:
                            values(it, g)
                            values(it, g + 1)
                        if g == 2:
                            inverse_deviation(it, LOOP)
                        if g == 3:
                            gelu(it, LOOP)
                        exponentials(it, g)
                    act.wait_ge(late_in, l * 64 + 64)
            it = STEPS
            nc.scalar.preload_act_table_set("natural_log_exp_and_others")
            exponentials(it, 0)
            turned(it, 0, TAIL)
            turned(it, 1, TAIL)
            squared_deviation(it)
            inverse_deviation(it, TAIL)
            gelu(it, TAIL)

        @block.gpsimd
        def _(pool):
            def square_sums(it, g, which):
                pool.wait_ge(s_sq, it * 8 + 2 * g + which + 1)
                pool.wait_ge(s_norm, it * 4 + g + 1)
                nc.gpsimd.tensor_tensor(sqs[:, which, :], sq[:, which, 0, :], sq[:, which, 1, :], ALU.add).then_inc(s_sqs, 1)

            def rotate(it, g, which):
                pool.wait_ge(s_rot, it * 8 + 2 * g + which + 3)
                for half in range(2):
                    ins = nc.gpsimd.tensor_tensor(m1[:, which, half, :], m1[:, which, half, :],
                                                  m2[:, which, 1 - half, :], ALU.add)
                ins.then_inc(s_add, 1)

            def less_max(it, g):
                pool.wait_ge(s_max, it * 4 + g + 1)
                x = sm[:, :, :].rearrange("p b (c j) -> p (b c) j", j=64)
                nc.gpsimd.tensor_tensor(x, x, mx[:, :].unsqueeze(2).broadcast_to([P, 16, 64]), ALU.subtract).then_inc(s_sub, 1)

            def normalise(it, g):
                pool.wait_ge(s_rsum, it * 4 + g + 1)
                x = pr[:, (g - 1) % 2, :, :].rearrange("p b (c j) -> p (b c) j", j=64)
                nc.gpsimd.tensor_tensor(x, x, rsum[:, :].unsqueeze(2).broadcast_to([P, 16, 64]), ALU.mult).then_inc(s_pr, 1)

            def affine(it):
                pool.wait_ge(s_xcr, it + 1)
                pool.sem_inc(held["pool"], 1)
                nc.gpsimd.tensor_scalar(xn[:, :], xc2[:, :], vec[:, 0:1], vec[:, 1:2], ALU.mult, ALU.add).then_inc(s_xn, 1)

            for t in (xm[:, :], xr[:, :], xs[:, :], qkn[:, :, :, :, :], pr[:, :, :, :], wo[:, :, :], w1[:, :],
                      w2[:, :, :], vec[:, :]):
                nc.gpsimd.memset(t, 0.0)
            for i, c in enumerate((2.0 ** -63, 1e-5, 0.5 * float(np.log(LN_SCALE)), 0.0)):
                ins = nc.gpsimd.memset(cst[:, i:i + 1], c)
            ins.then_inc(cleared, 1)
            for s, n in ((s_tab, 8), (s_proj, 8), (s_v, 4), (x_out, 32), (xr_in, 16), (q_in[1], 128), (vr_in[0], 48),
                         (vr_in[1], 48), (s_rot, 2), (s_sqs, 2), (s_norm, 1), (s_nf, 1), (s_sc, 1), (s_exp, 1), (s_pr, 1),
                         (s_pT, 1), (s_pv, 1), (s_oT, 2), (s_xo, 1), (s_w2, 1)):
                pool.sem_inc(s, n)
            pool.wait_ge(cleared, 2)
            with pool.Fori(0, DEPTH) as l:
                with pool.Fori(0, BATCH) as b:
                    it = l * BATCH + b
                    for g in range(NG):
                        square_sums(it, g, 0)
                        square_sums(it, g, 1)
                        rotate(it, g, 0)
                        rotate(it, g, 1)
                        less_max(it, g)
                        normalise(it, g)
                        if g == 2:
                            affine(it)
                    pool.wait_ge(late_in, l * 64 + 64)
            less_max(STEPS, 0)
            normalise(STEPS, 0)
            affine(STEPS)

        @block.vector
        def _(dve):
            def tables(l):
                dve.wait_ge(vecq_in, l * 16 + 16)
                for which in range(2):
                    for half in range(2):
                        q = vecq[:, 2 * which + half:2 * which + half + 1]
                        nc.vector.tensor_scalar(tab[:, which, 0, half, :], rope[:, 2 * which, :], q, None, ALU.mult)\
                            .then_inc(s_tab, 1)
                        nc.vector.tensor_scalar(tab[:, which, 1, half, :], rope[:, 2 * which + 1, :], q,
                                                -1.0 if half else 1.0, ALU.mult, ALU.mult).then_inc(s_tab, 1)
                dve.wait_ge(s_tab, l * 8 + 16)
                dve.sem_inc(held["dve"], 1)

            def rotate(it, g, which):
                dve.wait_ge(s_sq, it * 8 + 2 * g + which + 1)
                nc.vector.tensor_tensor(m1[:, which, :, :], pj[which][:, :, :], tab[:, which, 0, :, :], ALU.mult)
                nc.vector.tensor_tensor(m2[:, which, :, :], pj[which][:, :, :], tab[:, which, 1, :, :], ALU.mult)\
                    .then_inc(s_rot, 1)

            def mask(it, g, tasks):
                dve.wait_ge(s_sc, it * 4 + g + 2)
                dve.wait_ge(s_exp, it * 4 + g + 1)
                nc.vector.tensor_tensor(sm[:, :, :], bank(tasks, f"score{g}")[:, :, :],
                                        wmask[:, :].unsqueeze(1).broadcast_to([P, 2, SEQ]), ALU.add).then_inc(s_mask, 1)
                dve.wait_ge(s_mask, it * 4 + g + 1)
                nc.vector.tensor_reduce(mx[:, :], sm[:, :, :].rearrange("p b (c j) -> p (b c) j", j=64), AX.X, ALU.max)\
                    .then_inc(s_max, 1)

            def finish(it, g, which):
                if which == 0:
                    dve.wait_ge(s_rn, it * 4 + g + 1)
                    dve.wait_ge(q_in[(g + 1) % 2], it * 256 + 128 * (g // 2 + 1))
                dve.wait_ge(s_add, it * 8 + 2 * g + which + 1)
                nc.vector.scalar_tensor_tensor(out=nf[:, which, :, :], in0=rn[:, which, :].unsqueeze(1).broadcast_to([P, 2, SEQ]),
                                               scalar=1e12, in1=m1[:, which, :, :], op0=ALU.min, op1=ALU.mult)\
                    .then_inc(s_nf, 1)

            def denominators(it, g):
                dve.wait_ge(s_exp, it * 4 + g + 2)
                nc.vector.tensor_reduce(sums[:, :], pr[:, (g - 1) % 2, :, :].rearrange("p b (c j) -> p (b c) j", j=64),
                                        AX.X, ALU.add).then_inc(s_sum, 1)
                dve.wait_ge(s_sum, it * 4 + g + 1)
                dve.wait_ge(s_pr, it * 4 + g + 1)
                nc.vector.reciprocal(rsum[:, :], sums[:, :]).then_inc(s_rsum, 1)

            def weighted(it, g, tasks):
                dve.wait_ge(s_pv, it * 4 + g + 2)
                if g == 2:
                    dve.wait_ge(s_wo, it + 1)
                c = 2 * ((g - 2) % NG)
                for s in range(2):
                    nc.vector.tensor_copy(oT[:, c:c + 2, :].rearrange("p a (k s j) -> p a k s j", k=NBLK, s=2)[:, :, :, s, :],
                                          bank(tasks, f"weigh{g}")[:, s, :].rearrange("p (a k j) -> p a k j", a=2, k=NBLK))\
                        .then_inc(s_oT, 1)

            def residual(it, tasks):
                dve.wait_ge(s_wo, it + 1)
                dve.wait_ge(xr_in, it * 16 + 16)
                y = bank(tasks, "wo")
                for r, late in ((slice(0, 64), 0), (slice(64, P), 1)):
                    nc.vector.tensor_tensor(xm[r, late + WIN:late + SEQ], y[r, 0, 0:SEQ - WIN], xr[r, WIN:SEQ], ALU.add)
                    ins = nc.vector.tensor_tensor(xm[r, late:late + WIN], y[r, 0, SEQ - WIN:SEQ], xr[r, 0:WIN], ALU.add)
                ins.then_inc(s_xm, 1)
                dve.wait_ge(s_xm, it + 1)

            def centre(it, tasks):
                dve.wait_ge(s_mean, it + 1)
                nc.vector.tensor_tensor(xc[:, :], xm[:, 0:SEQ], bank(tasks, "mean")[:, 0, :], ALU.subtract).then_inc(s_xc, 1)
                dve.wait_ge(s_xc, it + 1)

            def scale(it):
                dve.wait_ge(s_rstd, it + 1)
                nc.vector.tensor_tensor(xc2[:, :], xc[:, :], rstd[:, :], ALU.mult).then_inc(s_xcr, 1)

            def gate(it, tasks):
                for c, n in enumerate(FCH):
                    dve.wait_ge(s_gl, it * 3 + c + 1)
                    dve.wait_ge(s_w1, it * 4 + 3 + c // 2)
                    nc.vector.scalar_tensor_tensor(out=gl[0:n, c, :], in0=bank(tasks, f"up{c // 2}")[0:n, c % 2, :],
                                                   scalar=vec[0:n, 3 + c:4 + c], in1=gl[0:n, c, :],
                                                   op0=ALU.add, op1=ALU.mult).then_inc(s_ug, 1)

            def finished(it, tasks):
                dve.wait_ge(s_w2, it + 2)
                dve.wait_ge(x_out, it * 16 + 16)
                for r, late in ((slice(0, 64), 0), (slice(64, P), 1)):
                    ins = nc.vector.scalar_tensor_tensor(out=xo[r, :], in0=bank(tasks, "out")[r, 0, :], scalar=vec[r, 2:3],
                                                         in1=xm[r, late:late + SEQ], op0=ALU.add, op1=ALU.add)
                ins.then_inc(s_xo, 1)

            for t in (v[:, :, SEQ:INNER], vr[:, :, :], oT[:, :, :]):
                ins = nc.vector.memset(t, 0.0)
            ins.then_inc(cleared, 1)
            dve.wait_ge(cleared, 2)
            dve.wait_ge(const_in, 80)
            with dve.Fori(0, DEPTH) as l:
                tables(l)
                with dve.Fori(0, BATCH) as b:
                    it = l * BATCH + b
                    for g in range(NG):
                        rotate(it, g, 0)
                        if g == 2:
                            centre(it, LOOP)
                        mask(it, g, LOOP)
                        rotate(it, g, 1)
                        finish(it, g, 0)
                        finish(it, g, 1)
                        if g == 3:
                            gate(it, LOOP)
                        denominators(it, g)
                        if g == 2:
                            scale(it)
                        weighted(it, g, LOOP)
                        if g == 1:
                            residual(it, LOOP)
                    finished(it, LOOP)
                    dve.wait_ge(late_in, l * 64 + 64)
            it = STEPS
            mask(it, 0, TAIL)
            denominators(it, 0)
            weighted(it, 0, TAIL)
            weighted(it, 1, TAIL)
            residual(it, TAIL)
            centre(it, TAIL)
            scale(it)
            gate(it, TAIL)
            finished(it, TAIL)


def stage3(nc, consts, x1d, hist, out):
    with ExitStack() as ctx:
        def sb(name, shape):
            return ctx.enter_context(nc.sbuf_tensor(name, shape, F32))

        ident = sb("ident3", [P, P])
        y = sb("y", [P, 2, SEQ])
        x1 = sb("x1_back", [P, 2, NBLK, P])
        o = sb("o", [P, 2, NBLK, P])
        pt = [ctx.enter_context(nc.psum_tensor(f"pt{i}", [P, SEQ], F32)) for i in range(2)]
        const_in = ctx.enter_context(nc.semaphore("const_in3"))
        loaded = [ctx.enter_context(nc.semaphore(f"loaded{i}")) for i in range(2)]
        turned = ctx.enter_context(nc.semaphore("turned"))
        added = ctx.enter_context(nc.semaphore("added"))
        stored = [ctx.enter_context(nc.semaphore(f"stored{i}")) for i in range(2)]
        block = ctx.enter_context(nc.Block())

        def tokens(t, i):
            return t[bass.ds(i, 1)].rearrange("a (k p) d -> p (a k) d", p=P)

        @block.sync
        def _(sp):
            sp.dma_start(ident[:, :], consts[:, C_ID:C_ID + P]).then_inc(const_in, 16)
            sp.sem_inc(added, 2)
            with sp.Fori(0, BATCH // 2) as c:
                for i in range(2):
                    b = c * 2 + i
                    sp.wait_ge(added, b + 1)
                    sp.dma_start(y[:, i, :], hist[bass.ds(b + STEPS, 1)].rearrange("a p n -> (a p) n")).then_inc(loaded[i], 16)
                    sp.dma_start(x1[:, i, :, :], tokens(x1d, b)).then_inc(loaded[i], 16)

        @block.tensor
        def _(pe):
            pe.wait_ge(const_in, 16)
            with pe.Fori(0, BATCH // 2) as c:
                for i in range(2):
                    b = c * 2 + i
                    pe.wait_ge(loaded[i], c * 32 + 32)
                    pe.wait_ge(added, b + 1)
                    for k in range(NBLK):
                        mm = pe.transpose(pt[i][:, k * P:(k + 1) * P], y[:, i, k * P:(k + 1) * P], ident[:, :])
                    mm.then_inc(turned, 1)

        @block.vector
        def _(dve):
            for i in range(2):
                dve.sem_inc(stored[i], 16)
            with dve.Fori(0, BATCH // 2) as c:
                for i in range(2):
                    b = c * 2 + i
                    dve.wait_ge(turned, b + 1)
                    dve.wait_ge(stored[i], c * 16 + 16)
                    nc.vector.tensor_tensor(o[:, i, :, :], pt[i][:, :].rearrange("p (k d) -> p k d", k=NBLK),
                                            x1[:, i, :, :], ALU.add).then_inc(added, 1)

        @block.scalar
        def _(act):
            with act.Fori(0, BATCH // 2) as c:
                for i in range(2):
                    b = c * 2 + i
                    act.wait_ge(added, b + 3)
                    act.dma_start(tokens(out, b), o[:, i, :, :]).then_inc(stored[i], 16)
            for i in range(2):
                act.wait_ge(stored[i], BATCH // 2 * 16 + 16)



def _constants():
    f = np.float32
    c = np.zeros((P, NCONST), f)
    i = np.arange(P)
    c[:, C_ID:C_ID + P] = np.eye(P)
    c[:, C_CM:C_CM + P] = np.where(i[None, :] <= i[:, None], 0.0, MASKED1)
    q = i % WIN
    par = i // WIN % 2
    j = np.arange(2 * WIN)
    ok = (j[None, :] >= q[:, None]) & (j[None, :] <= q[:, None] + WIN)
    m = np.where(ok, 0.0, MASKED)
    m = np.tile(m[:, None, :], (1, 2 * NBLK, 1))
    first = (par == 1)[:, None] & (j < WIN)[None, :]
    m[:, 2 * NBLK - 1, :] = np.where(first, MASKED, m[:, 2 * NBLK - 1, :])
    c[:, C_WM:C_WM + SEQ] = m.reshape(P, SEQ)
    c[:, C_BO:C_BO + P] = (i[:, None] // 32 == i[None, :] // 32)
    c[:, C_AV:C_AV + P] = 1.0 / P
    half = np.arange(0, DH2, 2, dtype=f)
    inv_freq = f(1.0) / np.power(f(10000.0), half / f(DH2))
    t = np.arange(SEQ, dtype=f)
    freqs = t[:, None] * inv_freq[None, :]
    base = (half + f(0.4 * DH2)) / f(1.4 * DH2)
    power = (t - f(SEQ // 2)) / f(WIN // 2)
    scale = np.power(base[None, :], power[:, None]).astype(f)
    cos, sin = np.cos(freqs), np.sin(freqs)
    for r, a in enumerate((cos * scale, sin * scale, cos * (f(1.0) / scale), sin * (f(1.0) / scale))):
        c[:, C_RO + r * SEQ:C_RO + (r + 1) * SEQ] = np.tile(a.T.astype(f), (P // HALF, 1))
    return c


def _layouts(w):
    a = {}
    W = w["L0_attn_Wqkv"].reshape(3, H1, DH1, P)
    qk = np.zeros((P, 2, NQ, QUAD, 32), np.float32)
    qk[..., :DH1] = W[:2].reshape(2, NQ, QUAD, DH1, P).transpose(4, 0, 1, 2, 3)
    a["w1qk"] = qk.reshape(P, 2, NQ, P)
    a["w1vo"] = np.stack([W[2].reshape(P, P).T, w["L0_attn_Wo"].T], axis=1)
    Wl = w["L0_ffn_Wqkv"].reshape(DEPTH, P, 3, NG, GRP, 2, HALF)
    q, k = (Wl[:, :, i].transpose(0, 1, 2, 4, 3, 5).reshape(DEPTH, P, NG, 2 * P) for i in range(2))
    v = Wl[:, :, 2].reshape(DEPTH, P, NG, 2 * P)
    a["wqkv"] = np.concatenate([q, k, v], axis=3).reshape(DEPTH, P, NG * NWQ)
    a["wod"] = w["L0_ffn_Wo"].reshape(DEPTH, INNER // P, P, P).transpose(0, 2, 1, 3)
    a["w1d"] = w["L0_ffn_W1"]
    w2 = np.zeros((DEPTH, 3 * P, P), np.float32)
    w2[:, :FFN] = w["L0_ffn_W2"]
    a["w2d"] = w2.reshape(DEPTH, 3, P, P).transpose(0, 2, 1, 3)
    vec = np.zeros((DEPTH, P, NVEC), np.float32)
    for i, n in enumerate(("ln_g", "ln_b", "b2")):
        vec[:, :, i] = w["L0_ffn_" + n]
    b1 = np.zeros((DEPTH, 2, 3 * P), np.float32)
    b1[:, :, :FFN] = w["L0_ffn_b1"].reshape(DEPTH, 2, FFN)
    vec[:, :, 3:9] = b1.reshape(DEPTH, 6, P).transpose(0, 2, 1)
    for i, n in enumerate(("q_scale", "k_scale")):
        s = w["L0_ffn_" + n].reshape(DEPTH, 2, HALF)
        vec[:, :, 9 + 2 * i:11 + 2 * i] = np.tile(s.transpose(0, 2, 1), (1, P // HALF, 1))
    a["vecd"] = vec
    return a


def kernel(**inputs):
    import concourse.bacc as bacc
    from concourse.bass_utils import run_bass_kernel_spmd

    w = {k: np.asarray(v) for k, v in inputs.items()}
    arrays = {"x": w["L0_attn_x"], "consts": _constants(), **_layouts(w)}
    arrays = {k: np.ascontiguousarray(v) for k, v in arrays.items()}
    nc = bacc.Bacc("TRN2", target_bir_lowering=False, num_devices=1)
    t = {k: nc.dram_tensor(k, a.shape, F32, kind="ExternalInput").ap() for k, a in arrays.items()}
    out = nc.dram_tensor("out", (BATCH, SEQ, P), F32, kind="ExternalOutput").ap()
    x1d = nc.dram_tensor("x1d", (BATCH, SEQ, P), F32, kind="Internal").ap()
    hist = nc.dram_tensor("hist", (HIST, P, SEQ), F32, kind="Internal").ap()
    stage1(nc, t["x"], t["consts"], t["w1qk"], t["w1vo"], x1d, hist)
    stage2(nc, t["consts"], t["wqkv"], t["wod"], t["w1d"], t["w2d"], t["vecd"], hist)
    stage3(nc, t["consts"], x1d, hist, out)
    r = run_bass_kernel_spmd(nc, [arrays], core_ids=[0])
    return r.results[0]["out"]
```
